# Optimizing a Trainium2 kernel written in Bass

```python
import numpy as np
import jax
import jax.numpy as jnp

def _softmax(x, axis=-1):
    return jax.nn.softmax(x, axis=axis)

def _gelu(x):
    return jax.nn.gelu(x, approximate=True)

def _silu(x):
    return jax.nn.silu(x)

def _sigmoid(x):
    return jax.nn.sigmoid(x)

def _layernorm(x, axis=-1, eps=1e-05):
    m = jnp.mean(x, axis=axis, keepdims=True)
    v = jnp.var(x, axis=axis, keepdims=True)
    return (x - m) / jnp.sqrt(v + eps)

def _scatter_add(tgt, idx, src, axis=0):
    return tgt.at[idx].add(src)

def _segment_sum(src, seg, n):
    return jax.ops.segment_sum(src, seg, n)
kernel_name = 'mk_gnn_resnorm_d1_gnn_r32_f652a3'

def setup_inputs(seed: int=0):
    np.random.seed(seed)
    _w = jnp.asarray

    def _rec_inputs():
        import jax
        import jax.numpy as jnp
        _gk = jax.random.key(seed)
        x = -0.0005121 + 1.001 * jax.random.normal(jax.random.fold_in(_gk, 1), (50000, 64), jnp.float32)
        src = jax.random.randint(jax.random.fold_in(_gk, 2), (50000,), 0, 50000, jnp.int32)
        dst = jnp.minimum((50000 * jax.random.uniform(jax.random.fold_in(_gk, 3), (50000,)) ** 2.0).astype(jnp.int32), 49999)
        _o = jnp.argsort(dst, stable=True)
        src = src[_o]
        dst = dst[_o]
        return (x, src, dst)
    x, src, dst = _rec_inputs()

    def _L0_gnn_setup():
        import jax, jax.numpy as jnp
        import numpy as np
        N = 50000
        E = 25000
        D = 64
        L = 3

        def _edge_conv(x, src, dst, w1, bb1, w2, bb2):
            xi = x[dst]
            xj = x[src]
            m = jnp.concatenate([xi, xj - xi], axis=-1)
            h = jax.nn.relu(m @ w1 + bb1) @ w2 + bb2
            agg = jax.ops.segment_sum(h, dst, num_segments=N)
            cnt = jax.ops.segment_sum(jnp.ones((dst.shape[0],), h.dtype), dst, num_segments=N)
            return agg / jnp.maximum(cnt, 1.0)[:, None]
        key = jax.random.key(seed)
        k_x, k_e, k_w1, k_w2 = jax.random.split(key, 4)
        s = 0.05
        x = jax.random.normal(k_x, (N, D), jnp.float32)
        edge_index = jax.random.randint(k_e, (2, E), 0, N)
        W1 = jax.random.normal(k_w1, (L, 2 * D, 4 * D), jnp.float32) * s
        b1 = jnp.zeros((L, 4 * D), jnp.float32)
        W2 = jax.random.normal(k_w2, (L, 4 * D, D), jnp.float32) * s
        b2 = jnp.zeros((L, D), jnp.float32)
        return {'x': x, 'edge_index': edge_index, 'W1': W1, 'b1': b1, 'W2': W2, 'b2': b2}
    _L0_gnn_all = _L0_gnn_setup()
    _L0_gnn_in = {k: v for k, v in _L0_gnn_all.items() if k in ('W1', 'b1', 'W2', 'b2')}
    del _L0_gnn_all
    return {'x': x, 'src': src, 'dst': dst, 'L0_gnn_W1': _L0_gnn_in['W1'], 'L0_gnn_b1': _L0_gnn_in['b1'], 'L0_gnn_W2': _L0_gnn_in['W2'], 'L0_gnn_b2': _L0_gnn_in['b2']}

def reference(x, src, dst, L0_gnn_W1, L0_gnn_b1, L0_gnn_W2, L0_gnn_b2):
    import jax
    import jax.numpy as jnp

    def _L0_gnn_ref(x, edge_index, W1, b1, W2, b2):
        import jax, jax.numpy as jnp
        import numpy as np
        N = 50000
        E = 25000
        D = 64
        L = 3

        def _edge_conv(x, src, dst, w1, bb1, w2, bb2):
            xi = x[dst]
            xj = x[src]
            m = jnp.concatenate([xi, xj - xi], axis=-1)
            h = jax.nn.relu(m @ w1 + bb1) @ w2 + bb2
            agg = jax.ops.segment_sum(h, dst, num_segments=N)
            cnt = jax.ops.segment_sum(jnp.ones((dst.shape[0],), h.dtype), dst, num_segments=N)
            return agg / jnp.maximum(cnt, 1.0)[:, None]
        src = edge_index[0]
        dst = edge_index[1]
        for l in range(L):
            x = _edge_conv(x, src, dst, W1[l], b1[l], W2[l], b2[l])
            if l < L - 1:
                x = jax.nn.relu(x)
        return x
    edge_index = jnp.stack([src, dst])
    x = _layernorm(x + _L0_gnn_ref(x, edge_index, L0_gnn_W1, L0_gnn_b1, L0_gnn_W2, L0_gnn_b2), axis=-1)
    return x

_drawn_inputs = setup_inputs


def setup_inputs(seed=0):
    import zlib

    import numpy as np

    out = dict(_drawn_inputs(seed))
    spreads = {'L0_gnn_b1': (0.0, 0.1), 'L0_gnn_b2': (0.0, 0.1)}
    factors = {'L0_gnn_W1': 2.722}
    for name, (base, spread) in spreads.items():
        noise = np.random.default_rng([zlib.crc32(name.encode()), seed]).standard_normal(out[name].shape)
        drawn = base * np.exp(spread * noise) if base else spread * noise
        out[name] = jnp.asarray(drawn.astype(out[name].dtype))
    for name, factor in factors.items():
        out[name] = (out[name] * factor).astype(out[name].dtype)
    return out
```

```python
from contextlib import ExitStack

import concourse.bass as bass
from concourse import mybir

F32 = mybir.dt.float32
BF16 = mybir.dt.bfloat16
I32 = mybir.dt.int32
I16 = mybir.dt.int16
U8 = mybir.dt.uint8
ALU = mybir.AluOpType
ACT = mybir.ActivationFunctionType
AX = mybir.AxisListType

P = 128
N = 50000
E = 50000
D = 64
HID = 256
HH = HID // P
L = 3
T = 4
G = T * P
NG = -(-max(N, E) // G)
R = NG * G
ZERO_ROW = R
W = D + 2
PITCH = 2 * D + 2
COUNT = D
SLOTS = 4
STEPS = NG // SLOTS
EPS = 1e-5

XT_SLOTS = 7
XT_ROUNDS = NG // XT_SLOTS
CHUNK = R // XT_ROUNDS
OH = 8
OH_ROUNDS = NG * T // OH


def uses(k):
    return -(-(NG - k) // SLOTS)


def program(nc, x, src, dst, dst_next, dst_prev, dst_line, w1, b1, w2, b2, out):
    ctx = ExitStack()
    with ctx:
        def sb(name, shape, dt=F32):
            return ctx.enter_context(nc.sbuf_tensor(name, shape, dt))

        def ps(name, shape):
            return ctx.enter_context(nc.psum_tensor(name, shape, F32))

        def sem(name):
            return ctx.enter_context(nc.semaphore(name))

        def sems(name, n):
            return [sem(f"{name}{k}") for k in range(n)]

        node_table = nc.dram_tensor("node_table", [R, W], F32).ap()
        xi_rows = nc.dram_tensor("xi_rows", [R, D], F32).ap()
        edge_rows = [nc.dram_tensor(f"edge_rows{l}", [R + 1, D], F32).ap() for l in range(L)]

        def by_group(table):
            return table[0:R, :].rearrange("(g p t) d -> g p (t d)", p=P, t=T)

        ident = sb("ident", [P, P])
        before = sb("before", [P, NG])
        iota_lo = sb("iota_lo", [P, G], I16)
        iota_hi = sb("iota_hi", [P, NG])
        w1_sb = sb("w1_sb", [P, L, HID])
        w1b_low = sb("w1b_low", [D, L, HID])
        w2_sb = sb("w2_sb", [P, L, HH, D + 1])
        b1_sb = sb("b1_sb", [P, L * HH])
        b2_sb = sb("b2_sb", [D + 1, L])
        eps = sb("eps", [P, 1])
        src_i = sb("src_i", [P, NG * T], I32)
        dst_i = sb("dst_i", [P, NG * T], I32)
        dst_row = sb("dst_row", [P, NG * T], I32)
        dst_nb = sb("dst_nb", [P, 2, NG * T], I32)
        run_end = sb("run_end", [P, 2, NG * T])
        end_of = sb("end_of", [P, NG * T], I32)
        start_of = sb("start_of", [P, NG * T], I32)
        same_run = sb("same_run", [D + 1, R], U8)
        same_run_back = sb("same_run_back", [D + 1, R + 1], U8)
        work = sb("work", [P, 2 * (CHUNK + 1)])
        line = [work[0:D + 1, k * (CHUNK + 1):(k + 1) * (CHUNK + 1)].bitcast(I32) for k in range(2)]
        taken = 0

        def tile_of_work(parts, *shape):
            nonlocal taken
            size = 1
            for s in shape:
                size *= s
            assert taken + size <= 2 * (CHUNK + 1)
            ap = work[0:parts, taken:taken + size]
            taken += size
            return ap.rearrange("p (a b) -> p a b", b=shape[-1]) if len(shape) == 2 else ap

        hi_i = sb("hi_i", [P, NG * T], I32)
        lo_i = sb("lo_i", [P, NG * T], I32)
        hi = sb("hi", [P, NG * T])
        lo = sb("lo", [P, NG * T])
        oh_hi = sb("oh_hi", [P, 2, OH // 2, NG], BF16)
        oh_lo = sb("oh_lo", [P, 2, OH // 2, G], BF16)
        zeros16 = sb("zeros16", [P, G], BF16)
        upto = sb("upto", [NG, G + 1])
        total = sb("total", [NG, 1])
        has = sb("has", [NG, G])
        place = sb("place", [NG, 2, G])
        place_t = sb("place_t", [P, 2, NG, T])
        end_row = sb("end_row", [P, NG * T], I32)
        xt = [sb(f"xt{k}", [P, T, W]) for k in range(XT_SLOTS)]
        idx = [sb(f"idx{k}", [P, T], I32) for k in range(SLOTS)]
        rows = [sb(f"rows{k}", [P, T, PITCH]) for k in range(SLOTS)]
        feat = [tile_of_work(P, G) for k in range(2)]
        hidden = [tile_of_work(P, HH, G) for k in range(2)]
        value = [tile_of_work(D + 1, G) for k in range(2)]
        sums = [tile_of_work(D + 1, G) for k in range(2)]
        res = [tile_of_work(P, T, D) for k in range(2)]
        sq = [tile_of_work(P, T, D) for k in range(2)]
        cen = [tile_of_work(P, T, D) for k in range(SLOTS)]
        inv = [sb(f"inv{k}", [P, 2, T]) for k in range(2)]
        made = [sb(f"made{k}", [P, T, D]) for k in range(SLOTS)]
        mean = [sb(f"mean{k}", [P, 2, T]) for k in range(2)]
        var = [sb(f"var{k}", [P, 3, T]) for k in range(2)]

        feat_ps = [ps(f"feat_ps{k}", [P, G]) for k in range(2)]
        hidden_ps = [ps(f"hidden_ps{k}", [P, HH, G]) for k in range(2)]
        value_ps = ps("value_ps", [D + 1, G])
        back_ps = ps("back_ps", [P, T, P])
        count_ps = hidden_ps[0][0:NG, 0, :]
        prefix_ps = hidden_ps[0][0:NG, 1, 0:1]
        place_ps = [hidden_ps[1][:, a, :].rearrange("p (t h) -> p t h", t=T)[:, :, 0:NG] for a in range(2)]

        edges_in = sem("edges_in")
        weights_in = sem("weights_in")
        zero_row_in = sem("zero_row_in")
        constants = sem("constants")
        index_made = sem("index_made")
        parts_cut = sem("parts_cut")
        parts_made = sem("parts_made")
        weights_made = sem("weights_made")
        zeros_made = sem("zeros_made")
        onehot_made = sem("onehot_made")
        onehot_used = sem("onehot_used")
        counted = sem("counted")
        totals_made = sem("totals_made")
        prefixed = sem("prefixed")
        upto_step = sem("upto_step")
        place_turned = sem("place_turned")
        place_made = sem("place_made")
        xt_loaded = sems("xt_loaded", XT_SLOTS)
        xt_filled = sem("xt_filled")
        xt_stored = sems("xt_stored", XT_SLOTS)
        line_loaded = sems("line_loaded", 2)
        line_used = sem("line_used")
        run_end_made = sem("run_end_made")
        idx_loaded = sems("idx_loaded", SLOTS)
        gathered = sems("gathered", SLOTS)
        near_loaded = sems("near_loaded", SLOTS)
        xi_stored = sems("xi_stored", SLOTS)
        turned = sem("turned")
        places_kept = sem("places_kept")
        feat_copied = sem("feat_copied")
        feat_filled = sem("feat_filled")
        hidden_made = sem("hidden_made")
        hidden_kept = sem("hidden_kept")
        value_made = sem("value_made")
        value_kept = sem("value_kept")
        summed = sem("summed")
        back = sem("back")
        inv_step = sem("inv_step")
        rows_made = sem("rows_made")
        made_stored = sems("made_stored", SLOTS)
        norm_step = sem("norm_step")
        rows_read = sem("rows_read")
        centred = sem("centred")
        squared = sem("squared")
        var_made = sem("var_made")
        root_made = sem("root_made")
        inv_made = sem("inv_made")

        passed = {e.engine: sem(name) for name, e in
                  (("passed_pool", nc.gpsimd), ("passed_sp", nc.sync), ("passed_dve", nc.vector))}

        block = ctx.enter_context(nc.Block())

        def wait(eng, semaphore, value):
            if not isinstance(value, int) or value > 0:
                eng.wait_ge(semaphore, value)

        def exists(n):
            return not isinstance(n, int) or 0 <= n < NG

        def over_groups(eng, step, lag=0, first=1):
            for i in range(first):
                for k in range(SLOTS):
                    step(i, k)
            with eng.Fori(first, STEPS) as i:
                for k in range(SLOTS):
                    step(i, k)
            for n in range(STEPS * SLOTS, NG + lag):
                step(n // SLOTS, n % SLOTS)

        def wait_alone(eng, semaphore, value):
            wait(eng, semaphore, value)
            if not isinstance(value, int):
                eng.sem_inc(passed[eng.engine], 1)

        def slot_of(k, lag):
            return (k - lag) % SLOTS

        def slot_uses(i, k, lag):
            return i if k >= lag else i - 1

        assert SLOTS == 4

        def place_of(l, n):
            return NG - 1 - n if l == 1 else n

        def cols(n):
            return bass.ds(n * T, T)

        def edge_range(l, n):
            return (same_run_back if l == 1 else same_run)[:, bass.ds(n * G, G)]

        def along(l, ap):
            return ap[:, ::-1] if l == 1 else ap

        @block.sync
        def _(sp):
            sp.dma_start(dst_i[:, :], dst).then_inc(edges_in, 16)
            sp.dma_start(src_i[:, :], src).then_inc(edges_in, 16)
            sp.dma_start(dst_nb[:, 0, :], dst_next).then_inc(edges_in, 16)
            sp.dma_start(dst_nb[:, 1, :], dst_prev).then_inc(edges_in, 16)
            sp.wait_ge(constants, 1)
            sp.dma_start(w1_sb[:, :, :], w1.rearrange("l k m -> k l m")).then_inc(weights_in, 16)
            sp.dma_start(w1b_low[:, :, :], w1[:, D:2 * D, :].rearrange("l k m -> k l m")).then_inc(weights_in, 16)
            for l in range(L):
                sp.dma_start(w2_sb[:, l, :, 0:D], w2[l, :, :].rearrange("(h k) m -> k h m", h=HH)).then_inc(weights_in, 16)
            sp.dma_start(b1_sb[:, :], b1).then_inc(weights_in, 16)
            sp.dma_start(b2_sb[0:D, :], b2).then_inc(weights_in, 16)
            for l in range(L):
                sp.dma_start(edge_rows[l][ZERO_ROW:ZERO_ROW + 1, :], made[0][0:1, 0, :]).then_inc(zero_row_in, 16)

            sp.wait_ge(index_made, 1)

            def first(i, k):
                n = i * SLOTS + k
                if exists(n):
                    wait(sp, xi_stored[k], 16 * i)
                    sp.dma_start(idx[k][:, :], dst_row[:, cols(n)]).then_inc(idx_loaded[k], 16)
                if exists(n - 2):
                    s = slot_of(k, 2)
                    sp.wait_ge(gathered[s], 16 * T * (slot_uses(i, k, 2) + 1))
                    sp.dma_start(by_group(xi_rows)[bass.ds(n - 2, 1), :, :].rearrange("a p (t d) -> p (a t) d", t=T),
                                 rows[s][:, :, 0:D]).then_inc(xi_stored[s], 16)

            over_groups(sp, first, lag=2)
            for k in range(SLOTS):
                sp.wait_ge(xi_stored[k], 16 * uses(k))
            for k in range(XT_SLOTS):
                sp.wait_ge(xt_stored[k], 16 * XT_ROUNDS)
            sp.wait_ge(zero_row_in, 16 * L)

            for l in range(L):
                near = by_group(xi_rows if l == 0 else edge_rows[l - 1])
                index = (src_i, end_of, start_of)[l]
                if l:
                    for k in range(SLOTS):
                        sp.wait_ge(made_stored[k], 16 * uses(k) * l)

                def load(i, k):
                    n = i * SLOTS + k
                    g = place_of(l, n)
                    wait_alone(sp, turned, l * NG + n - SLOTS + 1)
                    if l == 0:
                        wait_alone(sp, places_kept, n - SLOTS + 1)
                    if l == 1:
                        sp.wait_ge(places_kept, NG)
                    sp.dma_start(idx[k][:, :], index[:, cols(g)]).then_inc(idx_loaded[k], 16)
                    sp.dma_start(rows[k][:, :, 0:D],
                                 near[bass.ds(g, 1), :, :].rearrange("a p (t d) -> p (a t) d", t=T))\
                        .then_inc(near_loaded[k], 16)

                over_groups(sp, load)

            for k in range(SLOTS):
                sp.wait_ge(made_stored[k], 16 * uses(k) * L)

            def load_residual(i, k):
                n = i * SLOTS + k
                wait(sp, rows_read, n - SLOTS + 1)
                sp.dma_start(idx[k][:, :], end_row[:, cols(n)]).then_inc(idx_loaded[k], 16)
                sp.dma_start(rows[k][:, :, D:2 * D],
                             by_group(x)[bass.ds(n, 1), :, :].rearrange("a p (t d) -> p (a t) d", t=T))\
                    .then_inc(near_loaded[k], 16)

            over_groups(sp, load_residual)
            for k in range(SLOTS):
                sp.wait_ge(made_stored[k], 16 * uses(k) * (L + 1))

        @block.gpsimd
        def _(pool):
            pool.memset(w2_sb[:, :, :, :], 0.0)
            pool.memset(made[0][:, :, :], 0.0)
            pool.memset(ident[:, :], 0.0)
            pool.memset(before[:, :], 1.0)
            pool.memset(eps[:, :], EPS)
            pool.memset(zeros16[:, :], 0.0)
            pool.iota(iota_lo[:, :], [[1, G]], base=0, channel_multiplier=0, allow_small_or_imprecise_dtypes=True)
            pool.iota(iota_hi[:, :], [[1, NG]], base=0, channel_multiplier=0, allow_small_or_imprecise_dtypes=True)
            pool.drain().then_inc(constants, 1)
            pool.affine_select(out=ident[:, :], in_=ident[:, :], compare_op=ALU.not_equal, fill=1.0,
                               base=0, pattern=[[-1, P]], channel_multiplier=1).then_inc(constants, 1)
            pool.affine_select(out=before[:, :], in_=before[:, :], compare_op=ALU.is_gt, fill=0.0,
                               base=0, pattern=[[1, NG]], channel_multiplier=-1).then_inc(constants, 1)

            def gather(table, width, first_col, turn):
                last_row = pool.to_reg(table.shape[0] - 1)

                def step(i, k):
                    wait_alone(pool, idx_loaded[k], 16 * (turn * uses(k) + i + 1))
                    for t in range(T):
                        pool.indirect_dma_start(
                            out=rows[k][:, t, first_col:first_col + width], out_offset=None, in_=table,
                            in_offset=bass.IndirectOffsetOnAxis(ap=idx[k][:, t:t + 1], axis=0),
                            bounds_check=last_row).then_inc(gathered[k], 16)
                over_groups(pool, step)

            gather(x, D, 0, 0)
            gather(node_table, W, D, 1)
            gather(edge_rows[0], D, D, 2)
            gather(edge_rows[1], D, D, 3)
            gather(edge_rows[2], D, 0, 4)

        @block.tensor
        def _(pe):
            pe.wait_ge(constants, 1)
            pe.matmul(count_ps, zeros16[:, 0:NG], zeros16[:, :], start=True, stop=False)
            with pe.Fori(0, OH_ROUNDS) as i:
                for h in range(2):
                    pe.wait_ge(onehot_made, i * 2 + h + 1)
                    for t in range(OH // 2):
                        last = pe.matmul(count_ps, oh_hi[:, h, t, :], oh_lo[:, h, t, :], start=False, stop=False)
                    last.then_inc(onehot_used, 1)
            pe.matmul(count_ps, zeros16[:, 0:NG], zeros16[:, :], start=False, stop=True).then_inc(counted, 1)
            pe.wait_ge(constants, 3)
            pe.wait_ge(totals_made, 1)
            pe.matmul(prefix_ps, before[0:NG, :], total[:, :], start=True, stop=True).then_inc(prefixed, 1)
            pe.wait_ge(upto_step, 5)
            for a in range(2):
                for t in range(T):
                    last = pe.transpose(place_ps[a][:, t, :], place[:, a, t:G:T], ident[0:NG, 0:NG])
                last.then_inc(place_turned, 1)

            pe.wait_ge(weights_made, 2)
            pe.wait_ge(weights_in, 16 * (2 + L + 2))
            for l in range(L):
                at = l * NG

                def stages(i, k):
                    n = i * SLOTS + k
                    if exists(n):
                        pe.wait_ge(gathered[k], 16 * T * ((l + 1) * uses(k) + i + 1))
                        pe.wait_ge(near_loaded[k], 16 * (l * uses(k) + i + 1))
                        wait(pe, feat_copied, at + n - 1)
                        if l:
                            wait(pe, feat_filled, at - NG + n - 1)
                        for t in range(T):
                            last = pe.transpose(feat_ps[k % 2][:, t:G:T], rows[k][:, t, 0:2 * D], ident[:, :])
                        last.then_inc(turned, 1)
                    if exists(n - 1):
                        b = (k - 1) % 2
                        pe.wait_ge(feat_copied, at + n)
                        if l:
                            pe.wait_ge(feat_filled, at - NG + n)
                        wait(pe, hidden_kept, 2 * (at + n - 2))
                        for h in range(HH):
                            pe.matmul(hidden_ps[b][:, h, :], w1_sb[:, l, h * P:(h + 1) * P], feat[b][:, :],
                                      start=True, stop=True).then_inc(hidden_made, 1)
                    if exists(n - 2):
                        b = k % 2
                        pe.wait_ge(hidden_kept, 2 * (at + n - 1))
                        wait(pe, value_kept, at + n - 2)
                        for h in range(HH):
                            last = pe.matmul(value_ps[:, :], w2_sb[:, l, h, :], hidden[b][:, h, :],
                                             start=(h == 0), stop=(h == HH - 1))
                        last.then_inc(value_made, 1)
                    if exists(n - 3):
                        b = (k - 3) % 2
                        pe.wait_ge(summed, at + n - 2)
                        wait(pe, rows_made, at + n - 3)
                        for t in range(T):
                            last = pe.transpose(back_ps[:, t, 0:D + 1], sums[b][:, t:G:T], ident[0:D + 1, 0:D + 1])
                        last.then_inc(back, 1)

                over_groups(pe, stages, lag=3)

        @block.scalar
        def _(act):
            def table(i):
                for k in range(XT_SLOTS):
                    wait(act, xt_stored[k], 16 * i)
                    act.dma_start(xt[k][:, :, 0:D],
                                  by_group(x)[bass.ds(i * XT_SLOTS + k, 1), :, :].rearrange("a p (t d) -> p (a t) d", t=T))\
                        .then_inc(xt_loaded[k], 16)
                if isinstance(i, int) and i == 0:
                    for b in range(2):
                        load_line(b, b)
                    act.wait_ge(place_made, 1)
                for k in range(XT_SLOTS):
                    act.wait_ge(xt_loaded[k], 16 * (i + 1))
                    act.activation(xt[k][:, :, D:W].bitcast(I32).rearrange("p t a -> p a t"),
                                   place_t[:, :, bass.ds(i * XT_SLOTS + k, 1), :].rearrange("p a b t -> p a (b t)"),
                                   ACT.Copy).then_inc(xt_filled, 1)
                    act.wait_ge(xt_filled, i * XT_SLOTS + k + 1)
                    act.dma_start(node_table.rearrange("(g p t) d -> g p (t d)", p=P, t=T)[bass.ds(i * XT_SLOTS + k, 1), :, :]
                                  .rearrange("a p n -> p (a n)"),
                                  xt[k][:, :, :].rearrange("p t d -> p (t d)")).then_inc(xt_stored[k], 16)

            def load_line(c, b):
                act.dma_start(line[b][:, :], dst_line[:, bass.ds(c * CHUNK, CHUNK + 1)].broadcast_to([D + 1, CHUNK + 1]))\
                    .then_inc(line_loaded[b], 16)

            table(0)
            with act.Fori(1, XT_ROUNDS // 2) as j:
                for b in range(2):
                    act.wait_ge(line_used, j * 2 + b - 1)
                    load_line(j * 2 + b, b)
                    table(j * 2 + b - 1)
            table(XT_ROUNDS - 1)
            act.wait_ge(line_used, XT_ROUNDS + 1)

            for l in range(L):
                at = l * NG

                def stages(i, k):
                    n = i * SLOTS + k
                    if exists(n):
                        wait(act, hidden_made, 2 * (at + n - 1))
                        act.wait_ge(turned, at + n + 1)
                        p0 = D if l else 0
                        act.activation(feat[k % 2][p0:P, :], feat_ps[k % 2][p0:P, :], ACT.Copy)\
                            .then_inc(feat_copied, 1)
                    if exists(n - 1):
                        b = (k - 1) % 2
                        wait(act, value_made, at + n - 2)
                        for h in range(HH):
                            act.wait_ge(hidden_made, 2 * (at + n - 1) + h + 1)
                            act.activation(hidden[b][:, h, :], hidden_ps[b][:, h, :], ACT.Relu,
                                           bias=b1_sb[:, l * HH + h:l * HH + h + 1]).then_inc(hidden_kept, 1)
                    if exists(n - 2):
                        b = k % 2
                        wait(act, summed, at + n - 3)
                        act.wait_ge(value_made, at + n - 1)
                        act.activation(value[b][:, :], value_ps[:, :], ACT.Identity,
                                       bias=b2_sb[:, l:l + 1]).then_inc(value_kept, 1)
                    if exists(n - 4):
                        act.wait_ge(rows_made, at + n - 3)
                        act.dma_start(by_group(edge_rows[l])[bass.ds(place_of(l, n - 4), 1), :, :].rearrange("a p n -> p (a n)"),
                                      made[k][:, :, :].rearrange("p t d -> p (t d)")).then_inc(made_stored[k], 16)

                over_groups(act, stages, lag=4)

            def norm(i, k):
                n = i * SLOTS + k
                if exists(n):
                    wait(act, var_made, n - 1)
                    act.wait_ge(centred, n + 1)
                    act.activation(sq[k % 2][:, :, :], cen[k][:, :, :], ACT.Square).then_inc(squared, 1)
                if exists(n - 1):
                    b = (k - 1) % 2
                    act.wait_ge(var_made, n)
                    act.activation(var[b][:, 1, :], var[b][:, 0, :], ACT.Sqrt, bias=eps[:, :], scale=1.0 / D)\
                        .then_inc(root_made, 1)
                if exists(n - 3):
                    s = slot_of(k, 3)
                    act.wait_ge(rows_made, L * NG + n - 2)
                    act.dma_start(by_group(out)[bass.ds(n - 3, 1), :, :].rearrange("a p n -> p (a n)"),
                                  made[s][:, :, :].rearrange("p t d -> p (t d)")).then_inc(made_stored[s], 16)

            over_groups(act, norm, lag=3)

        @block.vector
        def _(dve):
            dve.memset(b2_sb[D:D + 1, :], 1.0).then_inc(weights_made, 1)
            dve.wait_ge(edges_in, 64)
            dve.tensor_scalar(dst_row[:, :], dst_i[:, :], N - 1, None, ALU.min).then_inc(index_made, 1)
            dve.tensor_scalar(hi_i[:, :], dst_i[:, :], 9, None, ALU.logical_shift_right).then_inc(parts_cut, 1)
            dve.tensor_scalar(lo_i[:, :], dst_i[:, :], G - 1, None, ALU.bitwise_and).then_inc(parts_cut, 1)
            dve.wait_ge(parts_cut, 2)
            dve.tensor_copy(hi[:, :], hi_i[:, :]).then_inc(parts_made, 1)
            dve.tensor_copy(lo[:, :], lo_i[:, :]).then_inc(parts_made, 1)
            for a in range(2):
                dve.tensor_tensor(run_end[:, a, :], dst_i[:, :], dst_nb[:, a, :], ALU.not_equal).then_inc(run_end_made, 1)
            dve.wait_ge(constants, 1)
            dve.wait_ge(parts_made, 2)
            q = OH // 2

            def onehot(i):
                for h in range(2):
                    wait(dve, onehot_used, i * 2 + h - 1)
                    dve.tensor_tensor(oh_hi[:, h, :, :], iota_hi[:, :].unsqueeze(1).broadcast_to([P, q, NG]),
                                      hi[:, bass.ds(i * OH + h * q, q)].unsqueeze(2).broadcast_to([P, q, NG]),
                                      ALU.is_equal)
                    for t in range(q):
                        last = dve.tensor_scalar(oh_lo[:, h, t, :], iota_lo[:, :], lo[:, bass.ds(i * OH + h * q + t, 1)],
                                                 None, ALU.is_ge)
                    last.then_inc(onehot_made, 1)

            onehot(0)
            with dve.Fori(1, OH_ROUNDS) as i:
                onehot(i)

            dve.wait_ge(counted, 1)
            dve.tensor_copy(total[:, :], count_ps[:, G - 1:G]).then_inc(totals_made, 1)
            dve.wait_ge(prefixed, 1)
            dve.tensor_copy(upto[:, 0:1], prefix_ps).then_inc(upto_step, 1)
            dve.wait_ge(upto_step, 1)
            dve.tensor_scalar(upto[:, 1:G + 1], count_ps, upto[:, 0:1], None, ALU.add).then_inc(upto_step, 1)
            dve.wait_ge(upto_step, 2)
            dve.tensor_tensor(has[:, :], upto[:, 1:G + 1], upto[:, 0:G], ALU.is_gt).then_inc(upto_step, 1)
            dve.wait_ge(upto_step, 3)
            for a, (first, off) in enumerate(((1, -1.0), (0, 0.0))):
                dve.scalar_tensor_tensor(place[:, a, :], upto[:, first:first + G], off - ZERO_ROW, has[:, :],
                                         ALU.add, ALU.mult).then_inc(upto_step, 1)
            for a in range(2):
                dve.wait_ge(place_turned, a + 1)
                dve.tensor_scalar(place_t[:, a, :, :].rearrange("p h t -> p t h"), place_ps[a], float(ZERO_ROW), None,
                                  ALU.add).then_inc(place_made, 1) if a else \
                    dve.tensor_scalar(place_t[:, a, :, :].rearrange("p h t -> p t h"), place_ps[a], float(ZERO_ROW), None,
                                      ALU.add).then_inc(upto_step, 1)
            dve.wait_ge(upto_step, 6)
            dve.tensor_copy(end_row[:, :], place_t[:, 0, :, :].rearrange("p h t -> p (h t)"))

            dve.wait_ge(weights_in, 16 * (2 + L + 2))
            dve.tensor_tensor(w1_sb[0:D, :, :], w1_sb[0:D, :, :], w1b_low[:, :, :], ALU.subtract).then_inc(weights_made, 1)

            with dve.Fori(0, XT_ROUNDS // 2) as j:
                for b in range(2):
                    dve.wait_ge(line_loaded[b], 16 * (j + 1))
                    dve.tensor_tensor(same_run[:, bass.ds((j * 2 + b) * CHUNK, CHUNK)], line[b][:, 1:CHUNK + 1],
                                      line[b][:, 0:CHUNK], ALU.is_equal)
                    dve.tensor_tensor(same_run_back[:, bass.ds(R + 1 - CHUNK - (j * 2 + b) * CHUNK, CHUNK)],
                                      line[b][:, 1:CHUNK + 1][:, ::-1], line[b][:, 0:CHUNK][:, ::-1], ALU.is_equal)\
                        .then_inc(line_used, 1)
            dve.memset(same_run_back[:, 0:1], 0).then_inc(line_used, 1)
            dve.wait_ge(line_used, XT_ROUNDS + 1)
            dve.wait_ge(run_end_made, 2)

            for l in range(L):
                at = l * NG

                def stages(i, k):
                    n = i * SLOTS + k
                    if exists(n) and l == 0:
                        dve.wait_ge(gathered[k], 16 * T * (uses(k) + i + 1))
                        dve.tensor_copy(end_of[:, cols(n)], rows[k][:, :, 2 * D].bitcast(I32))
                        dve.tensor_copy(start_of[:, cols(n)], rows[k][:, :, 2 * D + 1].bitcast(I32)).then_inc(places_kept, 1)
                    if exists(n) and l:
                        wait(dve, hidden_made, 2 * (at + n - 1))
                        dve.wait_ge(turned, at + n + 1)
                        wait(dve, feat_filled, at - NG + n)
                        carry = 0.0 if isinstance(n, int) and n == 0 else along(l, feat[(k - 1) % 2][0:D, :])[:, G - 1:G]
                        dve.tensor_tensor_scan(along(l, feat[k % 2][0:D, :]), edge_range(l, n)[0:D, :],
                                               along(l, feat_ps[k % 2][0:D, :]), carry, ALU.mult, ALU.add)\
                            .then_inc(feat_filled, 1)
                    if exists(n - 3):
                        b, s = (k - 3) % 2, slot_of(k, 3)
                        m = n - 3
                        g = place_of(l, m)
                        dve.wait_ge(back, at + m + 1)
                        dve.reciprocal(inv[b][:, 0, :], back_ps[:, :, COUNT]).then_inc(inv_step, 1)
                        wait_alone(dve, inv_step, 2 * (at + m) + 1)
                        if l < L - 1:
                            dve.tensor_tensor(inv[b][:, 1, :], inv[b][:, 0, :], run_end[:, l, cols(g)],
                                              ALU.mult).then_inc(inv_step, 1)
                        else:
                            dve.tensor_copy(inv[b][:, 1, :], inv[b][:, 0, :]).then_inc(inv_step, 1)
                        dve.wait_ge(inv_step, 2 * (at + m) + 2)
                        wait(dve, made_stored[s], 16 * (l * uses(s) + slot_uses(i, k, 3)))
                        scale = inv[b][:, 1, :].unsqueeze(2).broadcast_to([P, T, D])
                        if l < L - 1:
                            dve.scalar_tensor_tensor(made[s][:, :, :], back_ps[:, :, 0:D], 0.0, scale, ALU.max, ALU.mult)\
                                .then_inc(rows_made, 1)
                        else:
                            dve.tensor_tensor(made[s][:, :, :], back_ps[:, :, 0:D], scale, ALU.mult).then_inc(rows_made, 1)
                    if exists(n - 2):
                        m = n - 2
                        b = k % 2
                        wait(dve, back, at + m - 1)
                        dve.wait_ge(value_kept, at + m + 1)
                        wait(dve, summed, at + m)
                        carry = 0.0 if isinstance(m, int) and m == 0 else along(l, sums[1 - b][:, :])[:, G - 1:G]
                        dve.tensor_tensor_scan(along(l, sums[b][:, :]), edge_range(l, m), along(l, value[b][:, :]),
                                               carry, ALU.mult, ALU.add).then_inc(summed, 1)

                over_groups(dve, stages, lag=3, first=2 if l == 0 else 1)

            def norm(i, k):
                n = i * SLOTS + k
                if exists(n):
                    b = k % 2
                    dve.wait_ge(gathered[k], 16 * T * ((L + 1) * uses(k) + i + 1))
                    dve.wait_ge(near_loaded[k], 16 * (L * uses(k) + i + 1))
                    dve.tensor_tensor(res[b][:, :, :], rows[k][:, :, 0:D], rows[k][:, :, D:2 * D], ALU.add)\
                        .then_inc(rows_read, 1)
                    dve.wait_ge(rows_read, n + 1)
                    dve.tensor_reduce(mean[b][:, 0, :], res[b][:, :, :], AX.X, ALU.add).then_inc(norm_step, 1)
                    dve.wait_ge(norm_step, 2 * n + 1)
                    dve.tensor_scalar(mean[b][:, 1, :], mean[b][:, 0, :], 1.0 / D, None, ALU.mult).then_inc(norm_step, 1)
                    dve.wait_ge(norm_step, 2 * n + 2)
                    dve.tensor_tensor(cen[k][:, :, :], res[b][:, :, :],
                                      mean[b][:, 1, :].unsqueeze(2).broadcast_to([P, T, D]), ALU.subtract)\
                        .then_inc(centred, 1)
                if exists(n - 1):
                    b = (k - 1) % 2
                    dve.wait_ge(squared, n)
                    wait(dve, root_made, n - 2)
                    dve.tensor_reduce(var[b][:, 0, :], sq[b][:, :, :], AX.X, ALU.add).then_inc(var_made, 1)
                if exists(n - 2):
                    b, s = k % 2, slot_of(k, 2)
                    dve.wait_ge(root_made, n - 1)
                    dve.reciprocal(var[b][:, 2, :], var[b][:, 1, :]).then_inc(inv_made, 1)
                    dve.wait_ge(inv_made, n - 1)
                    dve.wait_ge(made_stored[s], 16 * (L * uses(s) + slot_uses(i, k, 2)))
                    dve.tensor_tensor(made[s][:, :, :], cen[s][:, :, :],
                                      var[b][:, 2, :].unsqueeze(2).broadcast_to([P, T, D]), ALU.mult)\
                        .then_inc(rows_made, 1)

            over_groups(dve, norm, lag=2)


def kernel(x, src, dst, L0_gnn_W1, L0_gnn_b1, L0_gnn_W2, L0_gnn_b2):
    import numpy as np
    import concourse.bacc as bacc
    from concourse.bass_utils import run_bass_kernel_spmd

    def pad(a, rows, fill):
        a = np.asarray(a)
        whole = np.full((rows,) + a.shape[1:], fill, a.dtype)
        whole[:a.shape[0]] = a
        return whole

    def by_tile(a):
        return np.ascontiguousarray(a.reshape(NG, P, T).transpose(1, 0, 2).reshape(P, NG * T))

    line = np.concatenate([np.full(1, -1, np.int32), pad(dst, R, N), np.full(1, N + 1, np.int32)])
    arrays = {
        "x_in": pad(x, R, 0),
        "src_in": by_tile(pad(src, R, 0)),
        "dst_in": by_tile(line[1:-1]),
        "dst_next_in": by_tile(line[2:]),
        "dst_prev_in": by_tile(line[:-2]),
        "dst_line_in": line.reshape(1, R + 2),
        "w1_in": np.ascontiguousarray(L0_gnn_W1),
        "b1_in": np.ascontiguousarray(np.asarray(L0_gnn_b1).reshape(L * HH, P).T),
        "w2_in": np.ascontiguousarray(L0_gnn_W2),
        "b2_in": np.ascontiguousarray(np.asarray(L0_gnn_b2).T),
    }
    nc = bacc.Bacc("TRN2", target_bir_lowering=False, num_devices=1)
    args = [nc.dram_tensor(name, a.shape, mybir.dt.from_np(a.dtype), kind="ExternalInput").ap()
            for name, a in arrays.items()]
    out = nc.dram_tensor("out_dram", (R, D), F32, kind="ExternalOutput").ap()
    program(nc, *args, out)
    result = run_bass_kernel_spmd(nc, [arrays], core_ids=[0])
    return result.results[0]["out_dram"][:N]
```

```python
from contextlib import ExitStack

import concourse.bass as bass
from concourse import mybir

F32 = mybir.dt.float32
BF16 = mybir.dt.bfloat16
I32 = mybir.dt.int32
I16 = mybir.dt.int16
U8 = mybir.dt.uint8
ALU = mybir.AluOpType
ACT = mybir.ActivationFunctionType
AX = mybir.AxisListType

P = 128
N = 50000
E = 50000
D = 64
HID = 256
HH = HID // P
L = 3
T = 4
G = T * P
NG = -(-max(N, E) // G)
R = NG * G
ZERO_ROW = R
W = D + 2
PITCH = 2 * D + 2
COUNT = D
SLOTS = 4
STEPS = NG // SLOTS
EPS = 1e-5

XT_SLOTS = 7
XT_ROUNDS = NG // XT_SLOTS
CHUNK = -(-(R + G) // XT_ROUNDS)
RUNS = XT_ROUNDS * CHUNK
OH = 8
OH_ROUNDS = NG * T // OH


def uses(k):
    return -(-(NG - k) // SLOTS)


def program(nc, x, src, dst, dst_next, dst_prev, dst_line, w1, b1, w2, b2, out):
    ctx = ExitStack()
    with ctx:
        def sb(name, shape, dt=F32):
            return ctx.enter_context(nc.sbuf_tensor(name, shape, dt))

        def ps(name, shape):
            return ctx.enter_context(nc.psum_tensor(name, shape, F32))

        def sem(name):
            return ctx.enter_context(nc.semaphore(name))

        def sems(name, n):
            return [sem(f"{name}{k}") for k in range(n)]

        node_table = nc.dram_tensor("node_table", [R, W], F32).ap()
        xi_rows = nc.dram_tensor("xi_rows", [R, D], F32).ap()
        edge_rows = [nc.dram_tensor(f"edge_rows{l}", [R + 1, D if l < L - 1 else 2 * D], F32).ap() for l in range(L)]

        def by_group(table):
            return table[0:R, :].rearrange("(g p t) d -> g p (t d)", p=P, t=T)

        ident = sb("ident", [P, P])
        before = sb("before", [P, NG])
        iota_lo = sb("iota_lo", [P, G], I16)
        iota_hi = sb("iota_hi", [P, NG])
        w1_sb = sb("w1_sb", [P, L, HID])
        w1b_low = sb("w1b_low", [D, L, HID])
        w2_sb = sb("w2_sb", [P, L, HH, D + 1])
        b1_sb = sb("b1_sb", [P, L * HH])
        b2_sb = sb("b2_sb", [D + 1, L])
        eps = sb("eps", [P, 1])
        src_i = sb("src_i", [P, NG * T], I32)
        dst_i = sb("dst_i", [P, NG * T], I32)
        dst_row = sb("dst_row", [P, NG * T], I32)
        dst_nb = sb("dst_nb", [P, 2, NG * T], I32)
        run_end = sb("run_end", [P, 2, NG * T])
        end_of = sb("end_of", [P, NG * T], I32)
        start_of = sb("start_of", [P, NG * T], I32)
        same_run = sb("same_run", [P, RUNS], U8)
        same_run_back = sb("same_run_back", [D + 1, RUNS + 1], U8)
        work = sb("work", [P, 2 * (CHUNK + 1)])
        line = [work[:, k * (CHUNK + 1):(k + 1) * (CHUNK + 1)].bitcast(I32) for k in range(2)]
        taken = 0

        def tile_of_work(parts, *shape):
            nonlocal taken
            size = 1
            for s in shape:
                size *= s
            assert taken + size <= 2 * (CHUNK + 1)
            ap = work[0:parts, taken:taken + size]
            taken += size
            return ap.rearrange("p (a b) -> p a b", b=shape[-1]) if len(shape) == 2 else ap

        hi_i = sb("hi_i", [P, NG * T], I32)
        lo_i = sb("lo_i", [P, NG * T], I32)
        hi = sb("hi", [P, NG * T])
        lo = sb("lo", [P, NG * T])
        oh_hi = sb("oh_hi", [P, 2, OH // 2, NG], BF16)
        made_all = sb("made_all", [P, SLOTS * T * 2 * D])
        made = [made_all[:, k * T * 2 * D:(k + 1) * T * 2 * D] for k in range(SLOTS)]
        oh_lo = made_all[:, :].bitcast(BF16).rearrange("p (a t g) -> p a t g", a=2, t=OH // 2)
        zeros16 = sb("zeros16", [P, G], BF16)
        upto = sb("upto", [NG, G + 1])
        total = sb("total", [NG, 1])
        has = sb("has", [NG, G])
        recip = sb("recip", [NG, G])
        facts = sb("facts", [NG, 4, G])
        lone = sb("lone", [NG, G // 2])
        place_t = sb("place_t", [P, 2, NG, T])
        own_scale = sb("own_scale", [P, NG * T])
        before_scale = sb("before_scale", [P, NG * 2])
        pair_row = sb("pair_row", [P, NG * 2], I32)
        xt = [sb(f"xt{k}", [P, T, W]) for k in range(XT_SLOTS)]
        idx = [sb(f"idx{k}", [P, T], I32) for k in range(SLOTS)]
        rows = [sb(f"rows{k}", [P, T, PITCH]) for k in range(SLOTS)]
        flat = [r[:, :, :].rearrange("p t w -> p (t w)") for r in rows]
        feat = [tile_of_work(P, G) for k in range(2)]
        hidden = [tile_of_work(P, HH, G) for k in range(2)]
        value = [tile_of_work(P, G) for k in range(2)]
        sums = [tile_of_work(P, G + 1) for k in range(2)]
        res = [tile_of_work(P, T, D) for k in range(SLOTS)]
        sq = tile_of_work(P, D)
        inv = [sb(f"inv{k}", [P, 2, T]) for k in range(2)]
        total_of = [sb(f"total_of{k}", [P, T]) for k in range(SLOTS)]
        neg_mean = [sb(f"neg_mean{k}", [P, T]) for k in range(SLOTS)]
        var = [sb(f"var{k}", [P, 3, T]) for k in range(2)]

        feat_ps = [ps(f"feat_ps{k}", [P, G]) for k in range(2)]
        hidden_ps = [ps(f"hidden_ps{k}", [P, HH, G]) for k in range(2)]
        value_ps = ps("value_ps", [D + 1, G])
        back_ps = ps("back_ps", [P, T, P])
        count_ps = hidden_ps[0][0:NG, 0, :]
        prefix_ps = hidden_ps[0][0:NG, 1, 0:1]
        facts_ps = [bank.rearrange("p (t h) -> p t h", t=T)[:, :, 0:NG] for bank in
                    (hidden_ps[1][:, 0, :], hidden_ps[1][:, 1, :], feat_ps[0][:, :], feat_ps[1][:, :])]

        dst_in = sem("dst_in")
        edges_in = sem("edges_in")
        weights_in = sem("weights_in")
        zero_row_in = sem("zero_row_in")
        constants = sem("constants")
        index_made = sem("index_made")
        parts_cut = sem("parts_cut")
        parts_made = sem("parts_made")
        weights_made = sem("weights_made")
        zeros_made = sem("zeros_made")
        onehot_made = sem("onehot_made")
        onehot_used = sem("onehot_used")
        counted = sem("counted")
        totals_made = sem("totals_made")
        prefixed = sem("prefixed")
        upto_step = sem("upto_step")
        facts_turned = sem("facts_turned")
        place_made = sem("place_made")
        facts_made = sem("facts_made")
        xt_loaded = sems("xt_loaded", XT_SLOTS)
        xt_filled = sem("xt_filled")
        xt_stored = sems("xt_stored", XT_SLOTS)
        line_loaded = sems("line_loaded", 2)
        line_used = sem("line_used")
        run_end_made = sem("run_end_made")
        idx_loaded = sems("idx_loaded", SLOTS)
        gathered = sems("gathered", SLOTS)
        near_loaded = sems("near_loaded", SLOTS)
        xi_stored = sems("xi_stored", SLOTS)
        turned = sem("turned")
        places_kept = sem("places_kept")
        feat_copied = sem("feat_copied")
        feat_filled = sem("feat_filled")
        hidden_made = sem("hidden_made")
        hidden_kept = sem("hidden_kept")
        value_made = sem("value_made")
        value_kept = sem("value_kept")
        summed = sem("summed")
        half_back = sem("half_back")
        back = sem("back")
        inv_step = sem("inv_step")
        rows_made = sem("rows_made")
        made_stored = sems("made_stored", SLOTS)
        behind_row_in = sem("behind_row_in")
        carried = sem("carried")
        behind_made = sem("behind_made")
        first_made = sem("first_made")
        pairs_added = sem("pairs_added")
        centred = sem("centred")
        squared = sem("squared")
        root_made = sem("root_made")
        inv_made = sem("inv_made")

        passed = {e.engine: sem(name) for name, e in
                  (("passed_pool", nc.gpsimd), ("passed_sp", nc.sync), ("passed_dve", nc.vector), ("passed_pe", nc.tensor))}

        block = ctx.enter_context(nc.Block())

        def wait(eng, semaphore, value):
            if not isinstance(value, int) or value > 0:
                eng.wait_ge(semaphore, value)

        def exists(n):
            return not isinstance(n, int) or 0 <= n < NG

        def over_groups(eng, step, lag=0, first=1):
            for i in range(first):
                for k in range(SLOTS):
                    step(i, k)
            with eng.Fori(first, STEPS) as i:
                for k in range(SLOTS):
                    step(i, k)
            for n in range(STEPS * SLOTS, NG + lag):
                step(n // SLOTS, n % SLOTS)

        def wait_alone(eng, semaphore, value):
            wait(eng, semaphore, value)
            if not isinstance(value, int):
                eng.sem_inc(passed[eng.engine], 1)

        def slot_of(k, lag):
            return (k - lag) % SLOTS

        def slot_uses(i, k, lag):
            return i if k >= lag else i - 1

        assert SLOTS == 4

        def place_of(l, n):
            return NG - 1 - n if l == 1 else n

        def cols(n):
            return bass.ds(n * T, T)

        def edge_range(l, n):
            return same_run_back[:, bass.ds(n * G + RUNS - R, G)] if l == 1 else same_run[:, bass.ds(n * G, G)]

        def along(l, ap):
            return ap[:, ::-1] if l == 1 else ap

        @block.sync
        def _(sp):
            sp.dma_start(dst_i[:, :], dst).then_inc(dst_in, 16)

            sp.wait_ge(index_made, 1)

            def first(i, k):
                n = i * SLOTS + k
                if exists(n):
                    wait(sp, xi_stored[k], 16 * i)
                    sp.dma_start(idx[k][:, :], dst_row[:, cols(n)]).then_inc(idx_loaded[k], 16)
                if exists(n - 2):
                    s = slot_of(k, 2)
                    sp.wait_ge(gathered[s], 16 * T * (slot_uses(i, k, 2) + 1))
                    sp.dma_start(by_group(xi_rows)[bass.ds(n - 2, 1), :, :].rearrange("a p (t d) -> p (a t) d", t=T),
                                 rows[s][:, :, 0:D]).then_inc(xi_stored[s], 16)

            over_groups(sp, first, lag=2)
            for l in range(L):
                near = by_group(xi_rows if l == 0 else edge_rows[l - 1])
                index = (src_i, end_of, start_of)[l]

                def load_index(i, k):
                    sp.dma_start(idx[k][:, :], index[:, cols(place_of(l, i * SLOTS + k))]).then_inc(idx_loaded[k], 16)

                def load_near(i, k):
                    sp.dma_start(rows[k][:, :, 0:D],
                                 near[bass.ds(place_of(l, i * SLOTS + k), 1), :, :].rearrange("a p (t d) -> p (a t) d", t=T))\
                        .then_inc(near_loaded[k], 16)

                if l == 0:
                    sp.wait_ge(edges_in, 48)
                    for k in range(SLOTS):
                        sp.wait_ge(gathered[k], 16 * T * uses(k))
                        load_index(0, k)
                    for k in range(SLOTS):
                        sp.wait_ge(xi_stored[k], 16 * uses(k))
                else:
                    if l == 1:
                        sp.wait_ge(places_kept, NG)
                    sp.wait_ge(turned, l * NG)
                    for k in range(SLOTS):
                        load_index(0, k)
                    for k in range(SLOTS):
                        sp.wait_ge(made_stored[k], 16 * uses(k) * l)
                for k in range(SLOTS):
                    load_near(0, k)
                if l == 1:
                    sp.dma_start(same_run[COUNT:COUNT + 1, :], same_run[COUNT + 1:COUNT + 2, :]).then_inc(behind_row_in, 16)

                def load(i, k):
                    if isinstance(i, int) and i == 0:
                        return
                    n = i * SLOTS + k
                    wait_alone(sp, turned, l * NG + n - SLOTS + 1)
                    if l == 0:
                        wait_alone(sp, places_kept, n - SLOTS + 1)
                    load_index(i, k)
                    load_near(i, k)

                over_groups(sp, load)

            def load_pair(i, k):
                n = i * SLOTS + k
                if isinstance(i, int) and i == 0:
                    sp.wait_ge(turned, L * NG)
                wait(sp, centred, n - SLOTS + 1)
                sp.dma_start(idx[k][:, 0:2], pair_row[:, bass.ds(n * 2, 2)]).then_inc(idx_loaded[k], 16)
                sp.dma_start(flat[k][:, T * D:2 * T * D], by_group(x)[bass.ds(n, 1), :, :].rearrange("a p n -> p (a n)"))\
                    .then_inc(near_loaded[k], 16)

            sp.wait_ge(facts_made, 3)
            over_groups(sp, load_pair)
            for k in range(SLOTS):
                sp.wait_ge(made_stored[k], 16 * uses(k) * (L + 1))

        @block.gpsimd
        def _(pool):
            pool.memset(w2_sb[:, :, :, :], 0.0)
            pool.memset(ident[:, :], 0.0)
            pool.memset(before[:, :], 1.0)
            pool.memset(eps[:, :], EPS)
            pool.memset(zeros16[:, :], 0.0)
            pool.iota(iota_lo[:, :], [[1, G]], base=0, channel_multiplier=0, allow_small_or_imprecise_dtypes=True)
            pool.iota(iota_hi[:, :], [[1, NG]], base=0, channel_multiplier=0, allow_small_or_imprecise_dtypes=True)
            pool.drain().then_inc(constants, 1)
            pool.affine_select(out=ident[:, :], in_=ident[:, :], compare_op=ALU.not_equal, fill=1.0,
                               base=0, pattern=[[-1, P]], channel_multiplier=1).then_inc(constants, 1)
            pool.affine_select(out=before[:, :], in_=before[:, :], compare_op=ALU.is_gt, fill=0.0,
                               base=0, pattern=[[1, NG]], channel_multiplier=-1).then_inc(constants, 1)

            def gather(table, turn, tiles, ready, places):
                last_row = pool.to_reg(table.shape[0] - 1)

                def step(i, k):
                    if isinstance(i, int) and i == 0:
                        ready(k)
                    wait_alone(pool, idx_loaded[k], 16 * (turn * uses(k) + i + 1))
                    for t in range(tiles):
                        pool.indirect_dma_start(
                            out=places(k, t), out_offset=None, in_=table,
                            in_offset=bass.IndirectOffsetOnAxis(ap=idx[k][:, t:t + 1], axis=0),
                            bounds_check=last_row).then_inc(gathered[k], 16)
                over_groups(pool, step)

            def nothing(k):
                pass

            def nodes_ready(k):
                if k == 0:
                    for j in range(XT_SLOTS):
                        pool.wait_ge(xt_stored[j], 16 * XT_ROUNDS)
                pool.wait_ge(xi_stored[k], 16 * uses(k))

            def edges_ready(l):
                def ready(k):
                    if k == 0:
                        pool.wait_ge(zero_row_in, 16 * L)
                        for j in range(SLOTS):
                            pool.wait_ge(made_stored[j], 16 * uses(j) * (l + 1))
                return ready

            def near_half(k, t):
                return rows[k][:, t, 0:D]

            def far_half(k, t):
                return rows[k][:, t, D:2 * D]

            def far_half_and_places(k, t):
                return rows[k][:, t, D:D + W]

            def pair(k, a):
                return flat[k][:, a * 2 * D:(a + 1) * 2 * D]

            gather(x, 0, T, nothing, near_half)
            gather(node_table, 1, T, nodes_ready, far_half_and_places)
            gather(edge_rows[0], 2, T, edges_ready(0), far_half)
            gather(edge_rows[1], 3, T, edges_ready(1), far_half)
            gather(edge_rows[2], 4, T // 2, edges_ready(2), pair)

        @block.tensor
        def _(pe):
            pe.wait_ge(constants, 1)
            pe.matmul(count_ps, zeros16[:, 0:NG], zeros16[:, :], start=True, stop=False)
            with pe.Fori(0, OH_ROUNDS) as i:
                for h in range(2):
                    pe.wait_ge(onehot_made, i * 2 + h + 1)
                    for t in range(OH // 2):
                        last = pe.matmul(count_ps, oh_hi[:, h, t, :], oh_lo[:, h, t, :], start=False, stop=False)
                    last.then_inc(onehot_used, 1)
            pe.matmul(count_ps, zeros16[:, 0:NG], zeros16[:, :], start=False, stop=True).then_inc(counted, 1)
            pe.wait_ge(constants, 3)
            pe.wait_ge(totals_made, 1)
            pe.matmul(prefix_ps, before[0:NG, :], total[:, :], start=True, stop=True).then_inc(prefixed, 1)
            for a, steps in enumerate((4, 5, 11, 11)):
                pe.wait_ge(upto_step, steps)
                for t in range(T):
                    last = pe.transpose(facts_ps[a][:, t, :], facts[:, a, t:G:T], ident[0:NG, 0:NG])
                last.then_inc(facts_turned, 1)

            pe.wait_ge(weights_made, 2)
            pe.wait_ge(weights_in, 16 * (2 + L + 2))
            for l in range(L):
                at = l * NG

                def stages(i, k):
                    n = i * SLOTS + k
                    if exists(n):
                        pe.wait_ge(gathered[k], 16 * T * ((l + 1) * uses(k) + i + 1))
                        pe.wait_ge(near_loaded[k], 16 * (l * uses(k) + i + 1))
                        wait(pe, feat_copied, at + n - 1)
                        if l:
                            wait(pe, feat_filled, at - NG + n - 1)
                        for t in range(T):
                            last = pe.transpose(feat_ps[k % 2][:, t:G:T], rows[k][:, t, 0:2 * D], ident[:, :])
                        last.then_inc(turned, 1)
                    if l == L - 1 and exists(n - 4):
                        wait(pe, rows_made, at + n - 4)
                        wait_alone(pe, summed, at + n - 3)
                        for t in range(T):
                            last = pe.transpose(back_ps[:, t, 0:D], sums[k % 2][0:D, 1 + t:G + 1:T], ident[0:D, 0:D])
                        last.then_inc(half_back, 1)
                    if exists(n - 1):
                        b = (k - 1) % 2
                        pe.wait_ge(feat_copied, at + n)
                        if l:
                            pe.wait_ge(feat_filled, at - NG + n)
                        wait(pe, hidden_kept, 2 * (at + n - 2))
                        for h in range(HH):
                            pe.matmul(hidden_ps[b][:, h, :], w1_sb[:, l, h * P:(h + 1) * P], feat[b][:, :],
                                      start=True, stop=True).then_inc(hidden_made, 1)
                    if l < L - 1 and exists(n - 3):
                        wait(pe, rows_made, at + n - 3)
                        pe.wait_ge(summed, at + n - 2)
                        for t in range(T):
                            last = pe.transpose(back_ps[:, t, 0:D + 1], sums[(k - 3) % 2][0:D + 1, 1 + t:G + 1:T],
                                                ident[0:D + 1, 0:D + 1])
                        last.then_inc(back, 1)
                    if l == L - 1 and exists(n - 4):
                        wait_alone(pe, half_back, n - 3)
                        wait_alone(pe, summed, at + n - 2)
                        for t in range(T):
                            last = pe.transpose(back_ps[:, t, D:2 * D], sums[1 - k % 2][D:P, 1 + t:G + 1:T], ident[D:P, D:P])
                        last.then_inc(back, 1)
                    if exists(n - 2):
                        b = k % 2
                        width = D + 1 if l < L - 1 else D
                        pe.wait_ge(hidden_kept, 2 * (at + n - 1))
                        wait(pe, value_kept, at + n - 2)
                        for h in range(HH):
                            last = pe.matmul(value_ps[0:width, :], w2_sb[:, l, h, 0:width], hidden[b][:, h, :],
                                             start=(h == 0), stop=(h == HH - 1))
                        last.then_inc(value_made, 1)

                over_groups(pe, stages, lag=3 if l < L - 1 else 4)

        @block.scalar
        def _(act):
            act.dma_start(src_i[:, :], src).then_inc(edges_in, 16)
            act.dma_start(dst_nb[:, 0, :], dst_next).then_inc(edges_in, 16)
            act.dma_start(dst_nb[:, 1, :], dst_prev).then_inc(edges_in, 16)
            act.dma_start(w1_sb[:, :, :], w1.rearrange("l k m -> k l m")).then_inc(weights_in, 16)
            act.dma_start(w1b_low[:, :, :], w1[:, D:2 * D, :].rearrange("l k m -> k l m")).then_inc(weights_in, 16)
            act.dma_start(b1_sb[:, :], b1).then_inc(weights_in, 16)
            act.dma_start(b2_sb[0:D, :], b2).then_inc(weights_in, 16)
            act.wait_ge(constants, 1)
            for l in range(L):
                act.dma_start(w2_sb[:, l, :, 0:D], w2[l, :, :].rearrange("(h k) m -> k h m", h=HH)).then_inc(weights_in, 16)
            for l in range(L):
                act.dma_start(edge_rows[l][ZERO_ROW:ZERO_ROW + 1, :], zeros16[0:1, 0:2 * edge_rows[l].shape[1]].bitcast(F32))\
                    .then_inc(zero_row_in, 16)

            def table(i):
                for k in range(XT_SLOTS):
                    wait(act, xt_stored[k], 16 * i)
                    act.dma_start(xt[k][:, :, 0:D],
                                  by_group(x)[bass.ds(i * XT_SLOTS + k, 1), :, :].rearrange("a p (t d) -> p (a t) d", t=T))\
                        .then_inc(xt_loaded[k], 16)
                if isinstance(i, int) and i == 0:
                    for b in range(2):
                        load_line(b, b)
                    act.wait_ge(place_made, 2)
                for k in range(XT_SLOTS):
                    act.wait_ge(xt_loaded[k], 16 * (i + 1))
                    act.activation(xt[k][:, :, D:W].bitcast(I32).rearrange("p t a -> p a t"),
                                   place_t[:, :, bass.ds(i * XT_SLOTS + k, 1), :].rearrange("p a b t -> p a (b t)"),
                                   ACT.Copy).then_inc(xt_filled, 1)
                    act.wait_ge(xt_filled, i * XT_SLOTS + k + 1)
                    act.dma_start(node_table.rearrange("(g p t) d -> g p (t d)", p=P, t=T)[bass.ds(i * XT_SLOTS + k, 1), :, :]
                                  .rearrange("a p n -> p (a n)"),
                                  xt[k][:, :, :].rearrange("p t d -> p (t d)")).then_inc(xt_stored[k], 16)

            def load_line(c, b):
                act.dma_start(line[b][0:D + 1, :], dst_line[:, bass.ds(c * CHUNK + G, CHUNK + 1)]
                              .broadcast_to([D + 1, CHUNK + 1])).then_inc(line_loaded[b], 16)
                act.dma_start(line[b][D + 1:P, :], dst_line[:, bass.ds(c * CHUNK, CHUNK + 1)]
                              .broadcast_to([P - D - 1, CHUNK + 1])).then_inc(line_loaded[b], 16)

            table(0)
            with act.Fori(1, XT_ROUNDS // 2) as j:
                for b in range(2):
                    act.wait_ge(line_used, j * 2 + b - 1)
                    load_line(j * 2 + b, b)
                    table(j * 2 + b - 1)
            table(XT_ROUNDS - 1)
            act.wait_ge(line_used, XT_ROUNDS)

            for l in range(L):
                at = l * NG

                def stages(i, k):
                    n = i * SLOTS + k
                    if exists(n):
                        wait(act, hidden_made, 2 * (at + n - 1))
                        act.wait_ge(turned, at + n + 1)
                        p0 = D if l else 0
                        act.activation(feat[k % 2][p0:P, :], feat_ps[k % 2][p0:P, :], ACT.Copy)\
                            .then_inc(feat_copied, 1)
                    if exists(n - 1):
                        b = (k - 1) % 2
                        wait(act, value_made, at + n - 2)
                        for h in range(HH):
                            act.wait_ge(hidden_made, 2 * (at + n - 1) + h + 1)
                            act.activation(hidden[b][:, h, :], hidden_ps[b][:, h, :], ACT.Relu,
                                           bias=b1_sb[:, l * HH + h:l * HH + h + 1]).then_inc(hidden_kept, 1)
                    if l == L - 1 and exists(n - 4):
                        wait(act, made_stored[k], 16 * (l * uses(k) + slot_uses(i, k, 4)))
                        act.wait_ge(back, at + n - 3)
                        act.activation(made[k][:, :], back_ps[:, :, :].rearrange("p t d -> p (t d)"), ACT.Copy)\
                            .then_inc(rows_made, 1)
                    if exists(n - 2):
                        b = k % 2
                        width = D + 1 if l < L - 1 else D
                        wait(act, summed, at + n - 3)
                        act.wait_ge(value_made, at + n - 1)
                        act.activation(value[b][0:width, :], value_ps[0:width, :], ACT.Identity,
                                       bias=b2_sb[0:width, l:l + 1]).then_inc(value_kept, 1)
                    lag = 3 if l < L - 1 else 4
                    if exists(n - lag):
                        s, width = slot_of(k, lag), edge_rows[l].shape[1]
                        act.wait_ge(rows_made, at + n - lag + 1)
                        act.dma_start(by_group(edge_rows[l])[bass.ds(place_of(l, n - lag), 1), :, :].rearrange("a p n -> p (a n)"),
                                      made[s][:, 0:T * width]).then_inc(made_stored[s], 16)

                over_groups(act, stages, lag=3 if l < L - 1 else 4)

            def norm(i, k):
                n = i * SLOTS + k
                if exists(n):
                    b = k % 2
                    wait(act, inv_made, n - 1)
                    act.wait_ge(centred, n + 1)
                    for t in range(T):
                        wait(act, squared, T * n + t)
                        act.activation(sq, res[k][:, t, :], ACT.Square, bias=neg_mean[k][:, t:t + 1],
                                       accum_out=var[b][:, 0, t:t + 1]).then_inc(squared, 1)
                if exists(n - 1):
                    b = (k - 1) % 2
                    act.wait_ge(squared, T * n)
                    act.activation(var[b][:, 1, :], var[b][:, 0, :], ACT.Sqrt, bias=eps[:, :], scale=1.0 / D)\
                        .then_inc(root_made, 1)
                if exists(n - 2):
                    s = slot_of(k, 2)
                    act.wait_ge(rows_made, L * NG + n - 1)
                    act.dma_start(by_group(out)[bass.ds(n - 2, 1), :, :].rearrange("a p n -> p (a n)"),
                                  made[s][:, 0:T * D]).then_inc(made_stored[s], 16)

            over_groups(act, norm, lag=2)

        @block.vector
        def _(dve):
            dve.memset(b2_sb[D:D + 1, :], 1.0).then_inc(weights_made, 1)
            dve.wait_ge(dst_in, 16)
            dve.tensor_scalar(dst_row[:, :], dst_i[:, :], N - 1, None, ALU.min).then_inc(index_made, 1)
            dve.tensor_scalar(hi_i[:, :], dst_i[:, :], 9, None, ALU.logical_shift_right).then_inc(parts_cut, 1)
            dve.tensor_scalar(lo_i[:, :], dst_i[:, :], G - 1, None, ALU.bitwise_and).then_inc(parts_cut, 1)
            dve.wait_ge(parts_cut, 2)
            dve.tensor_copy(hi[:, :], hi_i[:, :]).then_inc(parts_made, 1)
            dve.tensor_copy(lo[:, :], lo_i[:, :]).then_inc(parts_made, 1)
            dve.wait_ge(edges_in, 48)
            for a in range(2):
                dve.tensor_tensor(run_end[:, a, :], dst_i[:, :], dst_nb[:, a, :], ALU.not_equal).then_inc(run_end_made, 1)
            dve.wait_ge(constants, 1)
            dve.wait_ge(parts_made, 2)
            q = OH // 2

            def onehot(i):
                for h in range(2):
                    wait(dve, onehot_used, i * 2 + h - 1)
                    dve.tensor_tensor(oh_hi[:, h, :, :], iota_hi[:, :].unsqueeze(1).broadcast_to([P, q, NG]),
                                      hi[:, bass.ds(i * OH + h * q, q)].unsqueeze(2).broadcast_to([P, q, NG]),
                                      ALU.is_equal)
                    for t in range(q):
                        last = dve.tensor_scalar(oh_lo[:, h, t, :], iota_lo[:, :], lo[:, bass.ds(i * OH + h * q + t, 1)],
                                                 None, ALU.is_ge)
                    last.then_inc(onehot_made, 1)

            onehot(0)
            with dve.Fori(1, OH_ROUNDS) as i:
                onehot(i)

            dve.wait_ge(counted, 1)
            dve.tensor_copy(total[:, :], count_ps[:, G - 1:G]).then_inc(totals_made, 1)
            dve.wait_ge(prefixed, 1)
            dve.tensor_copy(upto[:, 0:1], prefix_ps).then_inc(upto_step, 1)
            dve.wait_ge(upto_step, 1)
            dve.tensor_scalar(upto[:, 1:G + 1], count_ps, upto[:, 0:1], None, ALU.add).then_inc(upto_step, 1)
            dve.wait_ge(upto_step, 2)
            dve.tensor_tensor(has[:, :], upto[:, 1:G + 1], upto[:, 0:G], ALU.is_gt).then_inc(upto_step, 1)
            dve.wait_ge(upto_step, 3)
            for a, (first, off) in enumerate(((1, -1.0), (0, 0.0))):
                dve.scalar_tensor_tensor(facts[:, a, :], upto[:, first:first + G], off - ZERO_ROW, has[:, :],
                                         ALU.add, ALU.mult).then_inc(upto_step, 1)
            for a in range(2):
                dve.wait_ge(facts_turned, a + 1)
                dve.tensor_scalar(place_t[:, a, :, :].rearrange("p h t -> p t h"), facts_ps[a], float(ZERO_ROW), None,
                                  ALU.add).then_inc(place_made, 1)
            dve.tensor_tensor(recip[:, :], upto[:, 1:G + 1], upto[:, 0:G], ALU.subtract).then_inc(upto_step, 1)
            dve.tensor_scalar(lone[:, :], has[:, 1:G:2], -1.0, 1.0, ALU.mult, ALU.add).then_inc(upto_step, 1)
            dve.wait_ge(upto_step, 7)
            dve.tensor_scalar(recip[:, :], recip[:, :], 1.0, None, ALU.max).then_inc(upto_step, 1)
            dve.tensor_tensor(facts[:, 3, 0:G:2], facts[:, 0, 0:G:2], lone[:, :], ALU.mult).then_inc(upto_step, 1)
            dve.wait_ge(upto_step, 9)
            dve.tensor_tensor(facts[:, 3, 0:G:2], facts[:, 3, 0:G:2], facts[:, 0, 1:G:2], ALU.add)
            dve.reciprocal(recip[:, :], recip[:, :]).then_inc(upto_step, 1)
            dve.wait_ge(upto_step, 10)
            dve.tensor_tensor(facts[:, 2, :], recip[:, :], has[:, :], ALU.mult).then_inc(facts_made, 1)
            dve.wait_ge(facts_made, 1)
            dve.tensor_tensor(facts[:, 3, 1:G:2], facts[:, 2, 0:G:2], has[:, 1:G:2], ALU.mult).then_inc(facts_made, 1)
            dve.wait_ge(facts_made, 2)
            dve.tensor_tensor(facts[:, 2, 0:G:2], facts[:, 2, 0:G:2], lone[:, :], ALU.mult).then_inc(upto_step, 1)
            dve.wait_ge(facts_turned, 4)
            dve.tensor_copy(own_scale.rearrange("p (h t) -> p t h", t=T), facts_ps[2])
            dve.tensor_copy(before_scale.rearrange("p (h t) -> p t h", t=2), facts_ps[3][:, 1:T:2, :])
            dve.tensor_scalar(pair_row.rearrange("p (h t) -> p t h", t=2), facts_ps[3][:, 0:T:2, :], float(ZERO_ROW), None,
                              ALU.add).then_inc(facts_made, 1)

            dve.wait_ge(weights_in, 16 * (2 + L + 2))
            dve.tensor_tensor(w1_sb[0:D, :, :], w1_sb[0:D, :, :], w1b_low[:, :, :], ALU.subtract).then_inc(weights_made, 1)

            with dve.Fori(0, XT_ROUNDS // 2) as j:
                for b in range(2):
                    dve.wait_ge(line_loaded[b], 32 * (j + 1))
                    dve.tensor_tensor(same_run[:, bass.ds((j * 2 + b) * CHUNK, CHUNK)], line[b][:, 1:CHUNK + 1],
                                      line[b][:, 0:CHUNK], ALU.is_equal)
                    dve.tensor_tensor(same_run_back[:, bass.ds(RUNS + 1 - CHUNK - (j * 2 + b) * CHUNK, CHUNK)],
                                      line[b][0:D + 1, 1:CHUNK + 1][:, ::-1], line[b][0:D + 1, 0:CHUNK][:, ::-1],
                                      ALU.is_equal).then_inc(line_used, 1)
            dve.wait_ge(line_used, XT_ROUNDS)
            dve.wait_ge(run_end_made, 2)

            for l in range(L):
                at = l * NG

                def stages(i, k):
                    n = i * SLOTS + k
                    if exists(n) and l == 0:
                        dve.wait_ge(gathered[k], 16 * T * (uses(k) + i + 1))
                        dve.tensor_copy(end_of[:, cols(n)], rows[k][:, :, 2 * D].bitcast(I32))
                        dve.tensor_copy(start_of[:, cols(n)], rows[k][:, :, 2 * D + 1].bitcast(I32)).then_inc(places_kept, 1)
                    if exists(n) and l:
                        wait(dve, hidden_made, 2 * (at + n - 1))
                        dve.wait_ge(turned, at + n + 1)
                        wait(dve, feat_filled, at - NG + n)
                        carry = 0.0 if isinstance(n, int) and n == 0 else along(l, feat[(k - 1) % 2][0:D, :])[:, G - 1:G]
                        dve.tensor_tensor_scan(along(l, feat[k % 2][0:D, :]), edge_range(l, n)[0:D, :],
                                               along(l, feat_ps[k % 2][0:D, :]), carry, ALU.mult, ALU.add)\
                            .then_inc(feat_filled, 1)
                    if l < L - 1 and exists(n - 3):
                        b, s = (k - 3) % 2, slot_of(k, 3)
                        m = n - 3
                        g = place_of(l, m)
                        dve.wait_ge(back, at + m + 1)
                        dve.reciprocal(inv[b][:, 0, :], back_ps[:, :, COUNT]).then_inc(inv_step, 1)
                        wait_alone(dve, inv_step, 2 * (at + m) + 1)
                        dve.tensor_tensor(inv[b][:, 1, :], inv[b][:, 0, :], run_end[:, l, cols(g)], ALU.mult)\
                            .then_inc(inv_step, 1)
                        dve.wait_ge(inv_step, 2 * (at + m) + 2)
                        wait(dve, made_stored[s], 16 * (l * uses(s) + slot_uses(i, k, 3)))
                        dve.scalar_tensor_tensor(made[s][:, 0:T * D].rearrange("p (t d) -> p t d", t=T), back_ps[:, :, 0:D], 0.0,
                                                 inv[b][:, 1, :].unsqueeze(2).broadcast_to([P, T, D]), ALU.max, ALU.mult)\
                            .then_inc(rows_made, 1)
                    m = n - 2
                    b = k % 2
                    start = isinstance(m, int) and m == 0
                    if l < L - 1 and exists(m):
                        wait(dve, back, at + m - 1)
                        dve.wait_ge(value_kept, at + m + 1)
                        wait(dve, summed, at + m)
                        carry = 0.0 if start else along(l, sums[1 - b][0:D + 1, 1:G + 1])[:, G - 1:G]
                        dve.tensor_tensor_scan(along(l, sums[b][0:D + 1, 1:G + 1]), edge_range(l, m)[0:D + 1, :],
                                               along(l, value[b][0:D + 1, :]), carry, ALU.mult, ALU.add).then_inc(summed, 1)
                    if l == L - 1 and (exists(m) or (isinstance(m, int) and m == NG)):
                        last = isinstance(m, int) and m == NG
                        p0, p1 = (D if last else 0), (D if start else P)
                        dve.wait_ge(back, at + m - 1)
                        if not last:
                            dve.wait_ge(value_kept, at + m + 1)
                        dve.wait_ge(summed, at + m)
                        if not start:
                            dve.wait_ge(behind_made, m)
                        dve.tensor_tensor_scan(sums[b][p0:p1, 1:G + 1], same_run[p0:p1, bass.ds(m * G, G)], value[b][p0:p1, :],
                                               0.0 if start else sums[1 - b][p0:p1, G:G + 1], ALU.mult, ALU.add)\
                            .then_inc(summed, 1)
                        if start:
                            dve.memset(sums[b][0:D, 0:1], 0.0).then_inc(carried, 1)
                            dve.memset(sums[b][D:P, G:G + 1], 0.0).then_inc(carried, 1)
                        elif not last:
                            dve.tensor_copy(sums[b][0:D, 0:1], sums[1 - b][0:D, G:G + 1]).then_inc(carried, 1)
                        if not last:
                            dve.wait_ge(summed, at + m + 1)
                            dve.wait_ge(carried, m + 2)
                            dve.scalar_tensor_tensor(value[1 - b][D:P, :], same_run[0:D, bass.ds(m * G, G)], 0.0,
                                                     sums[b][0:D, 0:G], ALU.is_equal, ALU.mult).then_inc(behind_made, 1)

                if l == L - 1:
                    dve.wait_ge(behind_row_in, 16)
                over_groups(dve, stages, lag=3, first=2 if l == 0 else 1)

            def norm(i, k):
                n = i * SLOTS + k
                if exists(n):
                    dve.wait_ge(gathered[k], 16 * T * (L + 1) * uses(k) + 16 * (T // 2) * (i + 1))
                    dve.wait_ge(near_loaded[k], 16 * (L * uses(k) + i + 1))
                    xs = [flat[k][:, (T + t) * D:(T + t + 1) * D] for t in range(T)]
                    own = [flat[k][:, (t // 2) * 2 * D:(t // 2) * 2 * D + D] for t in range(T)]
                    ahead = [flat[k][:, (t // 2) * 2 * D + D:(t // 2 + 1) * 2 * D] for t in range(T)]
                    for t in (0, 2, 1, 3):
                        dve.scalar_tensor_tensor(res[k][:, t, :], own[t], own_scale[:, bass.ds(n * T + t, 1)], xs[t],
                                                 ALU.mult, ALU.add, accum_out=total_of[k][:, t:t + 1] if t % 2 else None)\
                            .then_inc(first_made, 1)
                    dve.wait_ge(first_made, T * n + 2)
                    for t in (0, 2):
                        dve.scalar_tensor_tensor(res[k][:, t, :], ahead[t], before_scale[:, bass.ds(n * 2 + t // 2, 1)],
                                                 res[k][:, t, :], ALU.mult, ALU.add, accum_out=total_of[k][:, t:t + 1])\
                            .then_inc(pairs_added, 1)
                    dve.wait_ge(pairs_added, 2 * n + 2)
                    dve.wait_ge(first_made, T * (n + 1))
                    dve.tensor_scalar(neg_mean[k][:, :], total_of[k][:, :], -1.0 / D, None, ALU.mult)\
                        .then_inc(centred, 1)
                if exists(n - 2):
                    b, s = k % 2, slot_of(k, 2)
                    dve.wait_ge(root_made, n - 1)
                    dve.reciprocal(var[b][:, 2, :], var[b][:, 1, :]).then_inc(inv_made, 1)
                    dve.wait_ge(inv_made, n - 1)
                    dve.wait_ge(made_stored[s], 16 * (L * uses(s) + slot_uses(i, k, 2)))
                    for t in range(T):
                        last = dve.tensor_scalar(made[s][:, t * D:(t + 1) * D], res[s][:, t, :], neg_mean[s][:, t:t + 1],
                                                 var[b][:, 2, t:t + 1], ALU.add, ALU.mult)
                    last.then_inc(rows_made, 1)

            over_groups(dve, norm, lag=2)


def kernel(x, src, dst, L0_gnn_W1, L0_gnn_b1, L0_gnn_W2, L0_gnn_b2):
    import numpy as np
    import concourse.bacc as bacc
    from concourse.bass_utils import run_bass_kernel_spmd

    def pad(a, rows, fill):
        a = np.asarray(a)
        whole = np.full((rows,) + a.shape[1:], fill, a.dtype)
        whole[:a.shape[0]] = a
        return whole

    def by_tile(a):
        return np.ascontiguousarray(a.reshape(NG, P, T).transpose(1, 0, 2).reshape(P, NG * T))

    line = np.concatenate([np.full(G + 1, -1, np.int32), pad(dst, R, N), np.full(RUNS - R, N + 1, np.int32)])
    arrays = {
        "x_in": pad(x, R, 0),
        "src_in": by_tile(pad(src, R, 0)),
        "dst_in": by_tile(line[G + 1:G + 1 + R]),
        "dst_next_in": by_tile(line[G + 2:G + 2 + R]),
        "dst_prev_in": by_tile(line[G:G + R]),
        "dst_line_in": line.reshape(1, G + 1 + RUNS),
        "w1_in": np.ascontiguousarray(L0_gnn_W1),
        "b1_in": np.ascontiguousarray(np.asarray(L0_gnn_b1).reshape(L * HH, P).T),
        "w2_in": np.ascontiguousarray(L0_gnn_W2),
        "b2_in": np.ascontiguousarray(np.asarray(L0_gnn_b2).T),
    }
    nc = bacc.Bacc("TRN2", target_bir_lowering=False, num_devices=1)
    args = [nc.dram_tensor(name, a.shape, mybir.dt.from_np(a.dtype), kind="ExternalInput").ap()
            for name, a in arrays.items()]
    out = nc.dram_tensor("out_dram", (R, D), F32, kind="ExternalOutput").ap()
    program(nc, *args, out)
    result = run_bass_kernel_spmd(nc, [arrays], core_ids=[0])
    return result.results[0]["out_dram"][:N]
```
